# Optimizing a Trainium2 kernel written in Bass

```python
import numpy as np
import jax
import jax.numpy as jnp

def _softmax(x, axis=-1):
    return jax.nn.softmax(x, axis=axis)

def _gelu(x):
    return jax.nn.gelu(x, approximate=True)

def _silu(x):
    return jax.nn.silu(x)

def _sigmoid(x):
    return jax.nn.sigmoid(x)

def _layernorm(x, axis=-1, eps=1e-05):
    m = jnp.mean(x, axis=axis, keepdims=True)
    v = jnp.var(x, axis=axis, keepdims=True)
    return (x - m) / jnp.sqrt(v + eps)

def _scatter_add(tgt, idx, src, axis=0):
    return tgt.at[idx].add(src)

def _segment_sum(src, seg, n):
    return jax.ops.segment_sum(src, seg, n)
kernel_name = 'mk_cond_resid_d1_seqx_r2_ada8de'

def setup_inputs(seed: int=0):
    np.random.seed(seed)
    _w = jnp.asarray

    def _rec_inputs():
        import jax
        import jax.numpy as jnp
        _rk = jax.random.key(seed)
        x = -1.528e-05 + 0.9999 * jax.random.normal(jax.random.fold_in(_rk, 1), (8, 1024, 512), jnp.float32)
        _lenS = 1024 - jax.random.randint(jax.random.fold_in(_rk, 7), (8,), 0, max(1, 1024 // 4) + 1, jnp.int32)
        _lenS2 = 1024 - jax.random.randint(jax.random.fold_in(_rk, 8), (8,), 0, max(1, 1024 // 4) + 1, jnp.int32)
        cond_1024 = -0.00608245 + 1.00131 * jax.random.normal(jax.random.fold_in(_rk, 11), (8, 512), jnp.float32)
        return (x, cond_1024)
    x, cond_1024 = _rec_inputs()

    def _L0_cond_setup():
        import jax, jax.numpy as jnp
        import numpy as np
        LATENT = 512
        key = jax.random.key(seed)
        k1, k2, k3, k4 = jax.random.split(key, 4)
        B, T, D = (64, 256, LATENT)
        h_t = jax.random.normal(k1, (B, D), dtype=jnp.float32)
        z = jax.random.normal(k2, (B, T, D), dtype=jnp.float32)
        bound = 1.0 / np.sqrt(2 * D)
        W = jax.random.uniform(k3, (D, 2 * D), minval=-bound, maxval=bound, dtype=jnp.float32)
        b = jax.random.uniform(k4, (D,), minval=-bound, maxval=bound, dtype=jnp.float32)
        alpha = jnp.full((D,), 0.1, dtype=jnp.float32)
        return {'h_t': h_t, 'z': z, 'W': W, 'b': b, 'alpha': alpha}
    _L0_cond_all = _L0_cond_setup()
    _L0_cond_in = {k: v for k, v in _L0_cond_all.items() if k in ('W', 'b', 'alpha')}
    del _L0_cond_all
    return {'x': x, 'cond_1024': cond_1024, 'L0_cond_W': _L0_cond_in['W'], 'L0_cond_b': _L0_cond_in['b'], 'L0_cond_alpha': _L0_cond_in['alpha']}

def reference(x, cond_1024, L0_cond_W, L0_cond_b, L0_cond_alpha):
    import jax
    import jax.numpy as jnp

    def _L0_cond_ref(h_t, z, W, b, alpha):
        import jax, jax.numpy as jnp
        import numpy as np
        LATENT = 512
        D = h_t.shape[-1]
        Wh = W[:, :D]
        Wz = W[:, D:]
        leak = 1.0 - alpha

        def step(h, z_t):
            gate = jax.nn.sigmoid(h @ Wh.T + z_t @ Wz.T + b)
            h_new = jnp.tanh(h * leak + gate * z_t)
            return (h_new, h_new)
        _, hs = jax.lax.scan(step, h_t, jnp.swapaxes(z, 0, 1))
        return jnp.swapaxes(hs, 0, 1)
    x = x + _L0_cond_ref(cond_1024, x, L0_cond_W, L0_cond_b, L0_cond_alpha)
    return x

_drawn_inputs = setup_inputs


def setup_inputs(seed=0):
    import zlib

    import numpy as np

    out = dict(_drawn_inputs(seed))
    spreads = {'L0_cond_alpha': (0.10000000149011612, 0.6)}
    factors = {'cond_1024': 3.3, 'L0_cond_b': 28.538}
    for name, (base, spread) in spreads.items():
        noise = np.random.default_rng([zlib.crc32(name.encode()), seed]).standard_normal(out[name].shape)
        drawn = base * np.exp(spread * noise) if base else spread * noise
        out[name] = jnp.asarray(drawn.astype(out[name].dtype))
    for name, factor in factors.items():
        out[name] = (out[name] * factor).astype(out[name].dtype)
    return out
```

```python
import concourse.bass as bass
from concourse import mybir
from contextlib import ExitStack


def cond_resid_kernel(nc: bass.Bass, x, h0, wh, wz, bias, alpha, y):
    fp32 = mybir.dt.float32
    bf16 = mybir.dt.bfloat16
    ALU = mybir.AluOpType
    ACT = mybir.ActivationFunctionType
    AX = mybir.AxisListType

    P = 128
    B = 8
    COLS = h0.shape[1]
    CH = COLS // B
    T = x.shape[1] // COLS
    PARTS = 3
    BLK = 16
    BODY = 2 * BLK
    BLOCKS = T // BLK
    BODIES = T // BODY
    PIECE = BLK // CH
    assert CH == 4 and PIECE == CH and T % BODY == 0 and BODIES >= 2

    GROUPS = [[0], [1], [2, 3]]
    G = range(len(GROUPS))
    LAST = len(GROUPS) - 1
    GROUP_OF = {c: g for g, chunks in enumerate(GROUPS) for c in chunks}
    EARLY = [(j, k) for k in (0, 1) for j in range(CH)]
    LATE = [(j, k) for chunks in GROUPS for j in chunks for k in (2, 3)]
    ORDER = EARLY + LATE
    FINAL = {g: max(i for i, (j, _) in enumerate(ORDER) if GROUP_OF[j] == g) for g in G}

    SUM_AT, GATE_AT, ARG_AT = 128, 192, 320

    def cols(g):
        return slice(GROUPS[g][0] * B, (GROUPS[g][-1] + 1) * B)

    def width(g):
        return len(GROUPS[g]) * B

    ctx = ExitStack()
    with ctx:
        def sb(name, shape, dt):
            return ctx.enter_context(nc.sbuf_tensor(name, shape, dt))

        def pb(name):
            return ctx.enter_context(nc.psum_tensor(name, [P, 512], fp32))

        def sem(name):
            return ctx.enter_context(nc.semaphore(name))

        wh_f = sb("wh_f", [P, CH * CH * P], fp32)
        wh_p = sb("wh_p", [P, PARTS, CH * CH * P], bf16)
        wz_f = sb("wz_f", [P, CH * CH * P], fp32)
        h0_s = sb("h0_s", [P, COLS], fp32)
        bias_s = sb("bias_s", [P, CH], fp32)
        alpha_s = sb("alpha_s", [P, CH], fp32)
        leak = sb("leak", [P, COLS], fp32)
        ident = sb("ident", [P, P], bf16)
        xin = sb("xin", [P, 2, BLK, COLS], fp32)
        zu = sb("zu", [P, BODY, COLS, 2], fp32)
        zpart = sb("zpart", [P, 2, BLK, PARTS, COLS], fp32)
        hist = sb("hist", [P, BODY, PARTS, COLS], fp32)
        ybuf = sb("ybuf", [P, 2, BLK, COLS], fp32)

        bank = [pb(f"bank{g}") for g in G]
        inbank = [pb(f"inbank{i}") for i in range(2)]

        loaded_wz = sem("loaded_wz")
        loaded_c = sem("loaded_c")
        loaded_x = [sem(f"loaded_x{i}") for i in range(2)]
        stored_y = [sem(f"stored_y{i}") for i in range(2)]
        zeroed = sem("zeroed")
        ident_ready = sem("ident_ready")
        split_link = sem("split_link")
        wh_ready = sem("wh_ready")
        leak_ready = sem("leak_ready")
        banks_clear = sem("banks_clear")
        in_mm = sem("in_mm")
        in_full = sem("in_full")
        in_rest = sem("in_rest")
        in_split = sem("in_split")
        z_copied = sem("z_copied")
        leaked = sem("leaked")
        summed_y = sem("summed_y")
        gate_mm = [sem(f"gate_mm{g}") for g in G]
        pre_sum = [sem(f"pre_sum{g}") for g in G]
        gated = [sem(f"gated{g}") for g in G]
        mixed = [sem(f"mixed{g}") for g in G]
        h_full = [sem(f"h_full{g}") for g in G]
        h_rest = [sem(f"h_rest{g}") for g in G]
        h_parts = [sem(f"h_parts{g}") for g in G]

        block = ctx.enter_context(nc.Block())

        def upper(ap):
            view = ap.bitcast(bf16)
            return view[..., 1::2]

        def set_columns(g, chunk=None):
            sets = bank[g][:, 0:PARTS * width(g)].rearrange("p (a c) -> p a c", a=PARTS)
            if chunk is None:
                return sets
            at = (chunk - GROUPS[g][0]) * B
            return sets[:, :, at:at + B]

        def pair_columns(g, at):
            return bank[g][:, at:at + 2 * width(g)]

        def input_block(n_even, parity, s):
            m = (s + CH) % BLK
            return m // CH, m % CH, 1 if s + CH < BLK else 2

        def bodies(eng, emit):
            with eng.Fori(0, BODIES - 1) as n:
                emit(eng.snap(n * BODY), eng.snap(n * 16), False)
            emit(T - BODY, (BODIES - 1) * 16, True)

        def has_block(last, parity, ahead):
            return not last or parity + ahead < 2

        @block.sync
        def _(sp):
            sp.dma_start(xin[:, 0], x[:, 0:BLK * COLS].rearrange("p (t c) -> p t c", c=COLS)).then_inc(loaded_x[0], 16)
            sp.dma_start(wz_f[:], wz).then_inc(loaded_wz, 16)
            sp.dma_start(xin[:, 1], x[:, BLK * COLS:2 * BLK * COLS].rearrange("p (t c) -> p t c", c=COLS)).then_inc(loaded_x[1], 16)

            def emit(t, dmas, last):
                for parity in range(2):
                    t_blk = t + parity * BLK
                    if has_block(last, parity, 2):
                        sp.wait_ge(in_mm, t_blk + BLK)
                        sp.wait_ge(z_copied, t_blk + BLK)
                        sp.dma_start(xin[:, parity],
                                     x[:, bass.ds((t_blk + 2 * BLK) * COLS, BLK * COLS)].rearrange("p (t c) -> p t c", c=COLS))\
                            .then_inc(loaded_x[parity], 16)
                    sp.wait_ge(summed_y, t_blk + BLK)
                    sp.dma_start(y[:, bass.ds(t_blk * COLS, BLK * COLS)].rearrange("p (t c) -> p t c", c=COLS),
                                 ybuf[:, parity]).then_inc(stored_y[parity], 16)

            bodies(sp, emit)
            for parity in range(2):
                sp.wait_ge(stored_y[parity], 16 * (1 + BODIES))

        @block.gpsimd
        def _(pool):
            pool.memset(ident[:], 0.0).then_inc(zeroed, 1)
            for parity in range(2):
                pool.memset(ybuf[:, parity, 0], 0.0).then_inc(stored_y[parity], 16)
            pool.wait_ge(zeroed, 1)
            pool.affine_select(out=ident[:], in_=ident[:], compare_op=ALU.not_equal, fill=1.0, base=0,
                               pattern=[[-1, P]], channel_multiplier=1).then_inc(ident_ready, 1)

            def leak_times_h(slot_in, slot_out):
                pool.tensor_tensor(zu[:, slot_out, :, 1], hist[:, slot_in, 0, :], leak[:], ALU.mult).then_inc(leaked, 1)

            def copy_z(parity, piece):
                at = parity * BLK + piece * PIECE
                pool.tensor_copy(zu[:, at:at + PIECE, :, 0],
                                 xin[:, parity, piece * PIECE:(piece + 1) * PIECE, :]).then_inc(z_copied, 4)

            def split_input(parity, chunk, done_before):
                c = slice(chunk * B, (chunk + 1) * B)
                whole, rest, rest2 = (zpart[:, parity, :, a, c] for a in range(PARTS))
                pool.wait_ge(in_full, done_before + 4)
                pool.tensor_tensor(rest, whole, upper(whole), ALU.subtract).then_inc(in_rest, 4)
                pool.wait_ge(in_rest, done_before + 4)
                pool.tensor_tensor(rest2, rest, upper(rest), ALU.subtract).then_inc(in_split, 4)

            pool.wait_ge(loaded_x[0], 16)
            for piece in range(BLK // PIECE):
                copy_z(0, piece)
            pool.wait_ge(leak_ready, 1)
            for g in G:
                pool.wait_ge(h_full[g], 1)
            leak_times_h(BODY - 1, 0)
            for chunk in range(CH):
                split_input(0, chunk, 4 * chunk)

            def emit(t, dmas, last):
                for s_body in range(BODY):
                    parity, s = divmod(s_body, BLK)
                    if not (last and s_body == BODY - 1):
                        for g in G:
                            pool.wait_ge(h_full[g], t + s_body + 2)
                        leak_times_h(s_body, (s_body + 1) % BODY)
                    else:
                        for g in G:
                            pool.wait_ge(h_full[g], t + s_body + 2)
                    if s % PIECE == 0 and has_block(last, parity, 1):
                        split_input(1 - parity, s // PIECE, t + s_body + BLK)
                    if s % PIECE == 1 and has_block(last, parity, 1):
                        if s == 1:
                            pool.wait_ge(loaded_x[1 - parity], dmas + parity * 16 + 16)
                        copy_z(1 - parity, s // PIECE)
                    if s % PIECE == PIECE - 1:
                        q = s // PIECE
                        if q == 0:
                            pool.wait_ge(stored_y[parity], dmas + 16)
                        at = parity * BLK + q * PIECE
                        pool.tensor_tensor(ybuf[:, parity, q * PIECE:(q + 1) * PIECE, :],
                                           zu[:, at:at + PIECE, :, 0], hist[:, at:at + PIECE, 0, :],
                                           ALU.add).then_inc(summed_y, 4)

            bodies(pool, emit)

        @block.tensor
        def _(pe):
            def input_product(parity_x, chunk, k, done=in_mm):
                pe.matmul(inbank[chunk % 2][:, 0:BLK * B], wz_f[:, (k * CH + chunk) * P:(k * CH + chunk + 1) * P],
                          xin[:, parity_x, :, k * B:(k + 1) * B], start=(k == 0), stop=(k == CH - 1))\
                    .then_inc(done, 1)

            def open_group(g, parity, s):
                pe.matmul(set_columns(g), ident[:], upper(zpart[:, parity, s, :, cols(g)]),
                          start=True, stop=False, skip_group_check=True)

            pe.wait_ge(loaded_wz, 16)
            for n in range(BLK + CH):
                parity_x, m = divmod(n, BLK)
                chunk, k = divmod(m, CH)
                if n % BLK == 0:
                    pe.wait_ge(loaded_x[parity_x], 16)
                if k == 0 and n >= 2 * CH:
                    pe.wait_ge(in_full, n - CH)
                input_product(parity_x, chunk, k)
            pe.wait_ge(ident_ready, 1)
            pe.wait_ge(wh_ready, 1)
            pe.wait_ge(banks_clear, len(GROUPS))

            def emit(t, dmas, last):
                for s_body in range(BODY):
                    parity, s = divmod(s_body, BLK)
                    prev = (s_body - 1) % BODY
                    now = t + s_body
                    opened = set()
                    waited = set()
                    if s == 0:
                        pe.wait_ge(in_split, now + BLK)
                    for i, (j, k) in enumerate(ORDER):
                        g = GROUP_OF[j]
                        if g not in opened:
                            opened.add(g)
                            pe.wait_ge(h_full[g], now + 1)
                            open_group(g, parity, s)
                        if GROUP_OF[k] not in waited:
                            waited.add(GROUP_OF[k])
                            pe.wait_ge(h_parts[GROUP_OF[k]], now + 1)
                        for w in range(PARTS):
                            mm = pe.matmul(set_columns(g, j), wh_p[:, w, (k * CH + j) * P:(k * CH + j + 1) * P],
                                           upper(hist[:, prev, :, k * B:(k + 1) * B]),
                                           start=False, stop=(i == FINAL[g] and w == PARTS - 1),
                                           skip_group_check=True)
                        if i == FINAL[g]:
                            mm.then_inc(gate_mm[g], 1)
                    chunk, k, ahead = input_block(t, parity, s)
                    if has_block(last, parity, ahead):
                        parity_x = (parity + ahead) % 2
                        if k == 0:
                            pe.wait_ge(in_full, now + BLK)
                            if chunk == 0:
                                pe.wait_ge(loaded_x[parity_x], dmas + 32)
                        input_product(parity_x, chunk, k)

            bodies(pe, emit)

        @block.scalar
        def _(act):
            act.dma_start(wh_f[:], wh).then_inc(loaded_c, 16)
            act.dma_start(h0_s[:], h0).then_inc(loaded_c, 16)
            act.dma_start(bias_s[:], bias).then_inc(loaded_c, 16)
            act.dma_start(alpha_s[:], alpha).then_inc(loaded_c, 16)

            def evacuate(parity, chunk):
                nc.scalar.activation(zpart[:, parity, :, 0, chunk * B:(chunk + 1) * B],
                                     inbank[chunk % 2][:, 0:BLK * B].rearrange("p (t b) -> p t b", b=B),
                                     ACT.Identity, bias=bias_s[:, chunk:chunk + 1]).then_inc(in_full, 4)

            act.wait_ge(loaded_c, 64)
            for g in G:
                nc.scalar.copy(hist[:, BODY - 1, 0, cols(g)], h0_s[:, cols(g)]).then_inc(h_full[g], 1)
            for chunk in range(CH):
                act.wait_ge(in_mm, (chunk + 1) * CH)
                evacuate(0, chunk)

            def sigmoid(g, now):
                act.wait_ge(pre_sum[g], now + 1)
                nc.scalar.activation(pair_columns(g, GATE_AT)[:, 1::2], bank[g][:, SUM_AT:SUM_AT + width(g)],
                                     ACT.Sigmoid).then_inc(gated[g], 1)

            def tanh(g, s_body, now):
                act.wait_ge(mixed[g], now + 1)
                nc.scalar.activation(hist[:, s_body, 0, cols(g)], pair_columns(g, ARG_AT)[:, 1::2],
                                     ACT.Tanh).then_inc(h_full[g], 1)

            def emit(t, dmas, last):
                for s_body in range(BODY):
                    parity, s = divmod(s_body, BLK)
                    now = t + s_body
                    sigmoid(0, now)
                    sigmoid(1, now)
                    tanh(0, s_body, now)
                    sigmoid(2, now)
                    tanh(1, s_body, now)
                    tanh(2, s_body, now)
                    if s % PIECE == 0 and has_block(last, parity, 1):
                        act.wait_ge(in_mm, now + BLK + CH)
                        evacuate(1 - parity, s // PIECE)

            bodies(act, emit)

        @block.vector
        def _(dve):
            for g in G:
                dve.memset(pair_columns(g, GATE_AT), 0.0).then_inc(banks_clear, 1)
            dve.wait_ge(loaded_c, 64)
            link = 0
            dve.memset(leak[:], 0.0).then_inc(split_link, 1)
            link += 1
            dve.wait_ge(split_link, link)
            for j in range(CH):
                c = slice(j * B, (j + 1) * B)
                dve.tensor_scalar(leak[:, c], leak[:, c], alpha_s[:, j:j + 1], None, ALU.add).then_inc(split_link, 1)
                link += 1
            dve.wait_ge(split_link, link)
            dve.tensor_scalar(leak[:], leak[:], -1.0, 1.0, ALU.mult, ALU.add).then_inc(leak_ready, 1)

            def second_part(g, slot):
                whole = hist[:, slot, 0, cols(g)]
                dve.tensor_tensor(hist[:, slot, 1, cols(g)], whole, upper(whole), ALU.subtract).then_inc(h_rest[g], 1)

            def third_part(g, slot, now):
                dve.wait_ge(h_rest[g], now)
                rest = hist[:, slot, 1, cols(g)]
                dve.tensor_tensor(hist[:, slot, 2, cols(g)], rest, upper(rest), ALU.subtract).then_inc(h_parts[g], 1)

            for g in G:
                dve.wait_ge(h_full[g], 1)
                second_part(g, BODY - 1)
            for g in G:
                third_part(g, BODY - 1, 1)

            for w in range(PARTS):
                dve.tensor_copy(wh_p[:, w, :], upper(wh_f[:])).then_inc(split_link, 1)
                link += 1
                dve.wait_ge(split_link, link)
                if w < PARTS - 1:
                    dve.tensor_tensor(wh_f[:], wh_f[:], wh_p[:, w, :], ALU.subtract).then_inc(split_link, 1)
                    link += 1
                    dve.wait_ge(split_link, link)
            dve.memset(wh_f[:, 0:1], 0.0).then_inc(wh_ready, 1)

            def sum_sets(g, now):
                dve.wait_ge(gate_mm[g], now + 1)
                dve.tensor_reduce(bank[g][:, SUM_AT:SUM_AT + width(g)], set_columns(g).rearrange("p a c -> p c a"),
                                  AX.X, ALU.add).then_inc(pre_sum[g], 1)

            def mix(g, s_body, now):
                dve.wait_ge(gated[g], now + 1)
                if s_body % BLK == 0 and g == 0:
                    dve.wait_ge(z_copied, now + BLK)
                if g == 0:
                    dve.wait_ge(leaked, now + 1)
                dve.tensor_tensor_scan(pair_columns(g, ARG_AT), pair_columns(g, GATE_AT),
                                       zu[:, s_body, cols(g), :].rearrange("p c two -> p (c two)"),
                                       0.0, ALU.mult, ALU.add).then_inc(mixed[g], 1)

            def emit(t, dmas, last):
                for s_body in range(BODY):
                    now = t + s_body
                    sum_sets(0, now)
                    sum_sets(1, now)
                    mix(0, s_body, now)
                    sum_sets(2, now)
                    mix(1, s_body, now)
                    skip = last and s_body == BODY - 1
                    if not skip:
                        dve.wait_ge(h_full[0], now + 2)
                        second_part(0, s_body)
                    mix(2, s_body, now)
                    if not skip:
                        dve.wait_ge(h_full[1], now + 2)
                        second_part(1, s_body)
                        third_part(0, s_body, now + 2)
                        third_part(1, s_body, now + 2)
                        dve.wait_ge(h_full[2], now + 2)
                        second_part(2, s_body)
                        third_part(2, s_body, now + 2)

            bodies(dve, emit)


def kernel(x, cond_1024, L0_cond_W, L0_cond_b, L0_cond_alpha):
    import numpy as np
    import concourse.bacc as bacc
    from concourse.bass_utils import run_bass_kernel_spmd

    P = 128
    x, h0, W = (np.asarray(a) for a in (x, cond_1024, L0_cond_W))
    bias, alpha = np.asarray(L0_cond_b), np.asarray(L0_cond_alpha)
    B, T, D = x.shape
    CH = D // P

    def blocks(w):
        return np.ascontiguousarray(w.reshape(CH, P, CH, P).transpose(3, 2, 0, 1).reshape(P, CH * CH * P))

    arrays = {
        "x_dram": np.ascontiguousarray(x.reshape(B, T, CH, P).transpose(3, 1, 2, 0).reshape(P, T * CH * B)),
        "h0_dram": np.ascontiguousarray(h0.reshape(B, CH, P).transpose(2, 1, 0).reshape(P, CH * B)),
        "wh_dram": blocks(W[:, :D]),
        "wz_dram": blocks(W[:, D:]),
        "bias_dram": np.ascontiguousarray(bias.reshape(CH, P).T),
        "alpha_dram": np.ascontiguousarray(alpha.reshape(CH, P).T),
    }
    nc = bacc.Bacc("TRN2", target_bir_lowering=False, num_devices=1)
    args = [nc.dram_tensor(name, a.shape, mybir.dt.from_np(a.dtype), kind="ExternalInput").ap()
            for name, a in arrays.items()]
    y = nc.dram_tensor("y_dram", [P, T * CH * B], mybir.dt.float32, kind="ExternalOutput").ap()
    cond_resid_kernel(nc, *args, y)
    out = run_bass_kernel_spmd(nc, [arrays], core_ids=[0]).results[0]["y_dram"]
    return np.ascontiguousarray(np.asarray(out).reshape(P, T, CH, B).transpose(3, 1, 2, 0).reshape(B, T, D))
```

```python
import concourse.bass as bass
from concourse import mybir
from contextlib import ExitStack


def cond_resid_kernel(nc: bass.Bass, x, h0, wh, wz, bias, alpha, y):
    fp32 = mybir.dt.float32
    bf16 = mybir.dt.bfloat16
    ALU = mybir.AluOpType
    ACT = mybir.ActivationFunctionType
    AX = mybir.AxisListType

    P = 128
    B = 8
    COLS = h0.shape[1]
    CH = COLS // B
    T = x.shape[1] // COLS
    PARTS = 3
    BLK = 16
    BODY = 2 * BLK
    BODIES = T // BODY
    PIECE = BLK // CH
    assert CH == 4 and PIECE == CH and T % BODY == 0 and BODIES >= 2
    chunks = range(CH)

    def parts_of(*blocks):
        return [(j, k, w) for j, k in blocks for w in range(PARTS)]

    LEFT = [(2, 1, 2)]
    PASSES = ([p for p in parts_of((0, 0), (1, 0), (2, 0), (3, 0), (0, 1), (1, 1), (2, 1)) if p not in LEFT]
              + parts_of((0, 2), (0, 3), (1, 2), (1, 3)) + LEFT
              + parts_of((2, 2), (2, 3), (3, 1), (3, 2), (3, 3)))
    assert sorted(PASSES) == [(j, k, w) for j in chunks for k in chunks for w in range(PARTS)]
    FINAL = {j: max(i for i, p in enumerate(PASSES) if p[0] == j) for j in chunks}

    SUM_AT, GATE_AT, ARG_AT, AUX_COLS = 0, B, 3 * B, 5 * B

    def cols(j):
        return slice(j * B, (j + 1) * B)

    ctx = ExitStack()
    with ctx:
        def sb(name, shape, dt):
            return ctx.enter_context(nc.sbuf_tensor(name, shape, dt))

        def pb(name):
            return ctx.enter_context(nc.psum_tensor(name, [P, 512], fp32))

        def sem(name):
            return ctx.enter_context(nc.semaphore(name))

        w_whole = {m: sb(f"w{m}_whole", [P, CH, CH * P], fp32) for m in "zh"}
        w_rest = {m: sb(f"w{m}_rest", [P, CH, CH * P], fp32) for m in "zh"}
        w_part = {m: sb(f"w{m}_part", [P, PARTS, CH, CH * P], bf16) for m in "zh"}
        bias_s = sb("bias_s", [P, CH], fp32)
        alpha_s = sb("alpha_s", [P, CH], fp32)
        leak = sb("leak", [P, COLS], fp32)
        ident = sb("ident", [P, P], bf16)
        xpart = sb("xpart", [P, 2, PARTS, BLK, COLS], fp32)
        zu = sb("zu", [P, BODY, COLS, 2], fp32)
        zpart = sb("zpart", [P, 2, BLK, PARTS, COLS], fp32)
        hist = sb("hist", [P, BODY, PARTS, COLS], fp32)
        ybuf = sb("ybuf", [P, 2, BLK, COLS], fp32)
        aux_s = sb("aux_s", [P, AUX_COLS], fp32)

        set_bank = [pb(f"set_bank{j}") for j in chunks]
        aux = [aux_s if j == 2 else pb(f"aux_bank{j}") for j in chunks]
        in_bank = pb("in_bank")

        loaded_w = {m: [sem(f"loaded_w{m}{j}") for j in chunks] for m in "zh"}
        loaded_c = sem("loaded_c")
        loaded_x = [sem(f"loaded_x{i}") for i in range(2)]
        stored_y = [sem(f"stored_y{i}") for i in range(2)]
        zeroed = sem("zeroed")
        ident_ready = sem("ident_ready")
        w_rests = sem("w_rests")
        w_part01 = sem("w_part01")
        w_part2 = sem("w_part2")
        leak_link = sem("leak_link")
        aux_clear = sem("aux_clear")
        x_rest = sem("x_rest")
        x_split = sem("x_split")
        in_mm = sem("in_mm")
        in_full = sem("in_full")
        in_rest = sem("in_rest")
        in_split = sem("in_split")
        z_copied = sem("z_copied")
        leaked = sem("leaked")
        summed_y = sem("summed_y")
        gate_mm = [sem(f"gate_mm{j}") for j in chunks]
        pre_sum = [sem(f"pre_sum{j}") for j in chunks]
        gated = [sem(f"gated{j}") for j in chunks]
        mixed = [sem(f"mixed{j}") for j in chunks]
        h_full = [sem(f"h_full{j}") for j in chunks]
        h_rest = [sem(f"h_rest{j}") for j in chunks]
        h_split = [sem(f"h_split{j}") for j in chunks]

        block = ctx.enter_context(nc.Block())

        def upper(ap):
            return ap.bitcast(bf16)[..., 1::2]

        def part_sets(j):
            return set_bank[j][:, 0:PARTS * B].rearrange("p (a c) -> p a c", a=PARTS)

        def gate_pairs(j):
            return aux[j][:, GATE_AT:GATE_AT + 2 * B]

        def arg_pairs(j):
            return aux[j][:, ARG_AT:ARG_AT + 2 * B]

        def w_block(m, w, j, k):
            return w_part[m][:, w, j, k * P:(k + 1) * P]

        def x_steps(at):
            return bass.ds(at * COLS, BLK * COLS)

        def input_product(s):
            m = (s + CH) % BLK
            return m // CH, m % CH, 1 if s + CH < BLK else 2

        def has_block(last, parity, ahead):
            return not last or parity + ahead < 2

        def bodies(engine_type, eng, emit):
            with nc.Fori(0, BODIES - 1, engines=(engine_type,), hint_back_edge=True) as n:
                emit(eng.snap(n * BODY), eng.snap(n * 16), False)
            emit((BODIES - 1) * BODY, (BODIES - 1) * 16, True)

        @block.sync
        def _(sp):
            def load_x(t, parity):
                sp.dma_start(xpart[:, parity, 0], x[:, x_steps(t)].rearrange("p (t c) -> p t c", c=COLS))\
                    .then_inc(loaded_x[parity], 16)

            sp.dma_start(w_whole["z"][:, 0], wz[:, 0:CH * P]).then_inc(loaded_w["z"][0], 16)
            load_x(0, 0)
            for j in range(1, CH):
                sp.dma_start(w_whole["z"][:, j], wz[:, j * CH * P:(j + 1) * CH * P]).then_inc(loaded_w["z"][j], 16)
            load_x(BLK, 1)

            def emit(t, dmas, last):
                for parity in range(2):
                    t_blk = t + parity * BLK
                    if has_block(last, parity, 2):
                        sp.wait_ge(in_mm, t_blk + BLK)
                        sp.wait_ge(z_copied, t_blk + BLK)
                        load_x(t_blk + 2 * BLK, parity)
                    sp.wait_ge(summed_y, t_blk + 2 * BLK)
                    sp.dma_start(y[:, x_steps(t_blk)].rearrange("p (t c) -> p t c", c=COLS), ybuf[:, parity])\
                        .then_inc(stored_y[parity], 16)

            bodies(mybir.EngineType.SP, sp, emit)
            for parity in range(2):
                sp.wait_ge(stored_y[parity], 16 * (1 + BODIES))

        @block.gpsimd
        def _(pool):
            pool.memset(ident[:], 0.0).then_inc(zeroed, 1)
            for parity in range(2):
                pool.memset(ybuf[:, parity, 0], 0.0).then_inc(stored_y[parity], 16)
            pool.memset(ybuf[:, 0, 1], 0.0).then_inc(summed_y, BLK)
            pool.wait_ge(zeroed, 1)
            pool.affine_select(out=ident[:], in_=ident[:], compare_op=ALU.not_equal, fill=1.0, base=0,
                               pattern=[[-1, P]], channel_multiplier=1).then_inc(ident_ready, 1)

            def split_input(parity, j, a):
                before = zpart[:, parity, :, a - 1, cols(j)]
                pool.tensor_tensor(zpart[:, parity, :, a, cols(j)], before, upper(before), ALU.subtract)\
                    .then_inc(in_rest if a == 1 else in_split, 4)

            def add_y(parity, q):
                at = parity * BLK + q * PIECE
                pool.tensor_tensor(ybuf[:, parity, q * PIECE:(q + 1) * PIECE, :],
                                   zu[:, at:at + PIECE, :, 0], hist[:, at:at + PIECE, 0, :],
                                   ALU.add).then_inc(summed_y, 4)

            def emit(t, dmas, last):
                for s_body in range(BODY):
                    parity, s = divmod(s_body, BLK)
                    now = t + s_body
                    q, r = divmod(s, PIECE)
                    if last and s_body == BODY - 1:
                        for j in chunks:
                            pool.wait_ge(h_full[j], now + 1)
                    elif r != 2:
                        pool.wait_ge(leaked, now + 2)
                    if r == 0 and has_block(last, parity, 1):
                        pool.wait_ge(in_full, now + BLK + 4)
                        split_input(1 - parity, q, 1)
                    if r == 1 and has_block(last, parity, 1):
                        pool.wait_ge(in_rest, now + BLK + 3)
                        split_input(1 - parity, q, 2)
                    if r == PIECE - 1:
                        if q == 0:
                            pool.wait_ge(stored_y[parity], dmas + 16)
                        add_y(parity, q)

            bodies(mybir.EngineType.Pool, pool, emit)

        @block.tensor
        def _(pe):
            def multiply_input(parity, j, k):
                for w in range(PARTS):
                    for a in range(PARTS):
                        mm = pe.matmul(in_bank[:, 0:BLK * B], w_block("z", w, j, k),
                                       upper(xpart[:, parity, a, :, cols(k)]),
                                       start=(k == w == a == 0), stop=(k == CH - 1 and w == a == PARTS - 1))
                mm.then_inc(in_mm, 1)

            def open_step(slot):
                parity, s = divmod(slot, BLK)
                for j in chunks:
                    pe.matmul(part_sets(j), ident[:], upper(zpart[:, parity, s, :, cols(j)]),
                              start=True, stop=False, skip_group_check=True)

            for n in range(CH + 1):
                parity, j = divmod(n, CH)
                pe.wait_ge(w_part01, min(j + 1, CH))
                pe.wait_ge(w_part2, min(j + 1, CH))
                pe.wait_ge(x_split, BLK * (parity + 1))
                if n >= 1:
                    pe.wait_ge(in_full, 4 * n)
                for k in chunks:
                    multiply_input(parity, j, k)
            pe.wait_ge(ident_ready, 1)
            pe.wait_ge(in_split, BLK)
            open_step(0)
            pe.wait_ge(w_part01, 2 * CH)
            pe.wait_ge(w_part2, 2 * CH)

            def emit(t, dmas, last):
                for s_body in range(BODY):
                    parity, s = divmod(s_body, BLK)
                    before = (s_body - 1) % BODY
                    now = t + s_body
                    arrived = 0
                    for i, (j, k, w) in enumerate(PASSES):
                        if k == arrived:
                            arrived += 1
                            pe.wait_ge(h_split[k], now + 1)
                        mm = pe.matmul(part_sets(j), w_block("h", w, j, k), upper(hist[:, before, :, cols(k)]),
                                       start=False, stop=(i == FINAL[j]), skip_group_check=True)
                        if i == FINAL[j]:
                            mm.then_inc(gate_mm[j], 1)
                    j, k, ahead = input_product(s)
                    if has_block(last, parity, ahead):
                        if k == 0:
                            pe.wait_ge(in_full, now + BLK + 4)
                            if j == 0:
                                pe.wait_ge(x_split, now + CH + 2 * BLK)
                        multiply_input((parity + ahead) % 2, j, k)
                    if not (last and s_body == BODY - 1):
                        if s == BLK - 1:
                            pe.wait_ge(in_split, now + 1 + BLK)
                        for j in chunks:
                            pe.wait_ge(pre_sum[j], now + 1)
                        open_step((s_body + 1) % BODY)

            bodies(mybir.EngineType.PE, pe, emit)

        @block.scalar
        def _(act):
            act.dma_start(bias_s[:], bias).then_inc(loaded_c, 16)
            act.dma_start(alpha_s[:], alpha).then_inc(loaded_c, 16)
            act.dma_start(hist[:, BODY - 1, 0], h0).then_inc(loaded_c, 16)
            for j in chunks:
                act.dma_start(w_whole["h"][:, j], wh[:, j * CH * P:(j + 1) * CH * P]).then_inc(loaded_w["h"][j], 16)
            act.preload_act_table(ACT.Sigmoid)

            def evacuate(parity, j):
                nc.scalar.activation(zpart[:, parity, :, 0, cols(j)],
                                     in_bank[:, 0:BLK * B].rearrange("p (t b) -> p t b", b=B),
                                     ACT.Identity, bias=bias_s[:, j:j + 1]).then_inc(in_full, 4)

            def copy_z(parity, q):
                at = parity * BLK + q * PIECE
                nc.scalar.copy(zu[:, at:at + PIECE, :, 0],
                               xpart[:, parity, 0, q * PIECE:(q + 1) * PIECE, :]).then_inc(z_copied, 4)

            def copy_w(m, j):
                n = j + CH * "zh".index(m)
                act.wait_ge(loaded_w[m][j], 16)
                nc.scalar.copy(w_part[m][:, 0, j], upper(w_whole[m][:, j]))
                act.wait_ge(w_rests, n + 1)
                nc.scalar.copy(w_part[m][:, 1, j], upper(w_rest[m][:, j])).then_inc(w_part01, 1)

            for j in chunks:
                copy_w("z", j)
            act.wait_ge(loaded_c, 48)
            for n in range(CH + 1):
                act.wait_ge(in_mm, (n + 1) * CH)
                evacuate(n // CH, n % CH)
                if n < CH:
                    copy_w("h", n)
                    copy_z(0, n)

            def sigmoid(j, now):
                act.wait_ge(pre_sum[j], now + 1)
                nc.scalar.activation(gate_pairs(j)[:, 1::2], aux[j][:, SUM_AT:SUM_AT + B], ACT.Sigmoid)\
                    .then_inc(gated[j], 1)

            def tanh(j, slot, now):
                act.wait_ge(mixed[j], now + 1)
                nc.scalar.activation(hist[:, slot, 0, cols(j)], arg_pairs(j)[:, 1::2], ACT.Tanh)\
                    .then_inc(h_full[j], 1)

            def emit(t, dmas, last):
                for s_body in range(BODY):
                    parity, s = divmod(s_body, BLK)
                    now = t + s_body
                    sigmoid(0, now)
                    sigmoid(1, now)
                    sigmoid(2, now)
                    tanh(0, s_body, now)
                    sigmoid(3, now)
                    tanh(1, s_body, now)
                    tanh(2, s_body, now)
                    tanh(3, s_body, now)
                    j, k, ahead = input_product(s)
                    if k == CH - 1 and has_block(last, parity, ahead):
                        act.wait_ge(in_mm, now + 1 + BLK + CH)
                        evacuate((parity + ahead) % 2, j)
                    q, r = divmod(s, PIECE)
                    if r == 1 and has_block(last, parity, 1):
                        if q == 0:
                            act.wait_ge(loaded_x[1 - parity], dmas + parity * 16 + 16)
                        act.wait_ge(summed_y, now - 1 + PIECE)
                        copy_z(1 - parity, q)

            bodies(mybir.EngineType.Activation, act, emit)

        @block.vector
        def _(dve):
            def split_w(m, j):
                n = j + CH * "zh".index(m)
                dve.wait_ge(loaded_w[m][j], 16)
                dve.tensor_tensor(w_rest[m][:, j], w_whole[m][:, j], upper(w_whole[m][:, j]), ALU.subtract)\
                    .then_inc(w_rests, 1)
                dve.wait_ge(w_rests, n + 1)
                dve.tensor_tensor(w_part[m][:, 2, j], w_rest[m][:, j], upper(w_rest[m][:, j]), ALU.subtract)\
                    .then_inc(w_part2, 1)

            def split_x(parity, pieces, a):
                steps = slice(pieces[0] * PIECE, (pieces[-1] + 1) * PIECE)
                before = xpart[:, parity, a - 1, steps, :]
                dve.tensor_tensor(xpart[:, parity, a, steps, :], before, upper(before), ALU.subtract)\
                    .then_inc(x_rest if a == 1 else x_split, 4 * len(pieces))

            def second_part(j, slot):
                whole = hist[:, slot, 0, cols(j)]
                dve.tensor_tensor(hist[:, slot, 1, cols(j)], whole, upper(whole), ALU.subtract).then_inc(h_rest[j], 1)

            def third_part(j, slot, count):
                dve.wait_ge(h_rest[j], count)
                rest = hist[:, slot, 1, cols(j)]
                dve.tensor_tensor(hist[:, slot, 2, cols(j)], rest, upper(rest), ALU.subtract).then_inc(h_split[j], 1)

            def leak_times_h(slot_in, slot_out):
                dve.tensor_tensor(zu[:, slot_out, :, 1], hist[:, slot_in, 0, :], leak[:], ALU.mult).then_inc(leaked, 1)

            for j in chunks:
                dve.memset(gate_pairs(j), 0.0).then_inc(aux_clear, 1)
            dve.memset(leak[:], 0.0).then_inc(leak_link, 1)

            split_w("z", 0)
            for parity in range(2):
                dve.wait_ge(loaded_x[parity], 16)
                split_x(parity, chunks, 1)
                dve.wait_ge(x_rest, BLK * (parity + 1))
                split_x(parity, chunks, 2)
                if parity == 0:
                    for j in range(1, CH):
                        split_w("z", j)

            dve.wait_ge(loaded_c, 48)
            dve.wait_ge(leak_link, 1)
            for j in chunks:
                dve.tensor_scalar(leak[:, cols(j)], leak[:, cols(j)], alpha_s[:, j:j + 1], None, ALU.add)\
                    .then_inc(leak_link, 1)
            dve.wait_ge(leak_link, 1 + CH)
            dve.tensor_scalar(leak[:], leak[:], -1.0, 1.0, ALU.mult, ALU.add).then_inc(leak_link, 1)
            for j in chunks:
                second_part(j, BODY - 1)
            for j in chunks:
                third_part(j, BODY - 1, 1)
            dve.wait_ge(leak_link, 2 + CH)
            leak_times_h(BODY - 1, 0)

            for j in chunks:
                split_w("h", j)
                for a in (1, 2):
                    dve.wait_ge(in_full if a == 1 else in_rest, 4 * (j + 1))
                    before = zpart[:, 0, :, a - 1, cols(j)]
                    dve.tensor_tensor(zpart[:, 0, :, a, cols(j)], before, upper(before), ALU.subtract)\
                        .then_inc(in_rest if a == 1 else in_split, 4)
            dve.wait_ge(aux_clear, CH)

            def sum_sets(j, now):
                dve.wait_ge(gate_mm[j], now + 1)
                dve.tensor_reduce(aux[j][:, SUM_AT:SUM_AT + B], part_sets(j).rearrange("p a c -> p c a"),
                                  AX.X, ALU.add).then_inc(pre_sum[j], 1)

            def mix(j, slot, now):
                dve.wait_ge(gated[j], now + 1)
                if j == 0:
                    if slot % BLK == 0:
                        dve.wait_ge(z_copied, now + BLK)
                    dve.wait_ge(leaked, now + 1)
                dve.tensor_tensor_scan(arg_pairs(j), gate_pairs(j),
                                       zu[:, slot, cols(j), :].rearrange("p c two -> p (c two)"),
                                       0.0, ALU.mult, ALU.add).then_inc(mixed[j], 1)

            def emit(t, dmas, last):
                for slot in range(BODY):
                    parity, s = divmod(slot, BLK)
                    now = t + slot
                    end = last and slot == BODY - 1

                    def rest(j):
                        if not end:
                            dve.wait_ge(h_full[j], now + 1)
                            second_part(j, slot)

                    def third(j):
                        if not end:
                            third_part(j, slot, now + 2)

                    sum_sets(0, now)
                    sum_sets(1, now)
                    sum_sets(2, now)
                    mix(0, slot, now)
                    sum_sets(3, now)
                    mix(1, slot, now)
                    mix(2, slot, now)
                    rest(0)
                    mix(3, slot, now)
                    third(0)
                    rest(1)
                    rest(2)
                    third(1)
                    rest(3)
                    third(2)
                    third(3)
                    if not end:
                        leak_times_h(slot, (slot + 1) % BODY)
                    q, r = divmod(s, PIECE)
                    if has_block(last, parity, 2) and q in (1, 2):
                        if q == 1 and r == 0:
                            dve.wait_ge(loaded_x[parity], dmas + 32)
                        if q == 2:
                            dve.wait_ge(x_rest, now - s + 2 * BLK + 4 * (r + 1))
                        split_x(parity, [r], q)

            bodies(mybir.EngineType.DVE, dve, emit)


def kernel(x, cond_1024, L0_cond_W, L0_cond_b, L0_cond_alpha):
    import numpy as np
    import concourse.bacc as bacc
    from concourse.bass_utils import run_bass_kernel_spmd

    P = 128
    x, h0, W = (np.asarray(a) for a in (x, cond_1024, L0_cond_W))
    bias, alpha = np.asarray(L0_cond_b), np.asarray(L0_cond_alpha)
    B, T, D = x.shape
    CH = D // P

    def blocks(w):
        return np.ascontiguousarray(w.reshape(CH, P, CH, P).transpose(3, 0, 2, 1).reshape(P, CH * CH * P))

    arrays = {
        "x_dram": np.ascontiguousarray(x.reshape(B, T, CH, P).transpose(3, 1, 2, 0).reshape(P, T * CH * B)),
        "h0_dram": np.ascontiguousarray(h0.reshape(B, CH, P).transpose(2, 1, 0).reshape(P, CH * B)),
        "wh_dram": blocks(W[:, :D]),
        "wz_dram": blocks(W[:, D:]),
        "bias_dram": np.ascontiguousarray(bias.reshape(CH, P).T),
        "alpha_dram": np.ascontiguousarray(alpha.reshape(CH, P).T),
    }
    nc = bacc.Bacc("TRN2", target_bir_lowering=False, num_devices=1)
    args = [nc.dram_tensor(name, a.shape, mybir.dt.from_np(a.dtype), kind="ExternalInput").ap()
            for name, a in arrays.items()]
    y = nc.dram_tensor("y_dram", [P, T * CH * B], mybir.dt.float32, kind="ExternalOutput").ap()
    cond_resid_kernel(nc, *args, y)
    out = run_bass_kernel_spmd(nc, [arrays], core_ids=[0]).results[0]["y_dram"]
    return np.ascontiguousarray(np.asarray(out).reshape(P, T, CH, B).transpose(3, 1, 2, 0).reshape(B, T, D))
```

```python
import concourse.bass as bass
from concourse import mybir
from contextlib import ExitStack


def cond_resid_kernel(nc: bass.Bass, x, h0, wh, wz, bias, alpha, y):
    fp32 = mybir.dt.float32
    bf16 = mybir.dt.bfloat16
    ALU = mybir.AluOpType
    ACT = mybir.ActivationFunctionType
    AX = mybir.AxisListType

    P = 128
    B = 8
    COLS = h0.shape[1]
    CH = COLS // B
    T = x.shape[1] // COLS
    PARTS = 3
    BLK = 16
    BODY = 2 * BLK
    BODIES = T // BODY
    WARM_UP = 40
    PIECE = BLK // CH
    assert CH == 4 and PIECE == CH and T % BODY == 0 and BODIES >= 2
    chunks = range(CH)

    def parts_of(*blocks):
        return [(j, k, w) for j, k in blocks for w in range(PARTS)]

    LEFT = [(2, 1, 2)]
    PASSES = ([p for p in parts_of((0, 0), (1, 0), (2, 0), (3, 0), (0, 1), (1, 1), (2, 1)) if p not in LEFT]
              + parts_of((0, 2), (0, 3), (1, 2), (1, 3)) + LEFT
              + parts_of((2, 2), (2, 3), (3, 1), (3, 2), (3, 3)))
    assert sorted(PASSES) == [(j, k, w) for j in chunks for k in chunks for w in range(PARTS)]
    FINAL = {j: max(i for i, p in enumerate(PASSES) if p[0] == j) for j in chunks}

    SUM_AT, GATE_AT, ARG_AT, AUX_COLS = 0, B, 3 * B, 5 * B

    def cols(j):
        return slice(j * B, (j + 1) * B)

    ctx = ExitStack()
    with ctx:
        def sb(name, shape, dt):
            return ctx.enter_context(nc.sbuf_tensor(name, shape, dt))

        def pb(name):
            return ctx.enter_context(nc.psum_tensor(name, [P, 512], fp32))

        def sem(name):
            return ctx.enter_context(nc.semaphore(name))

        w_whole = {m: sb(f"w{m}_whole", [P, CH, CH * P], fp32) for m in "zh"}
        w_rest = {m: sb(f"w{m}_rest", [P, CH, CH * P], fp32) for m in "zh"}
        w_part = {m: sb(f"w{m}_part", [P, PARTS, CH, CH * P], bf16) for m in "zh"}
        bias_s = sb("bias_s", [P, CH], fp32)
        alpha_s = sb("alpha_s", [P, CH], fp32)
        leak = sb("leak", [P, COLS], fp32)
        ident = sb("ident", [P, P], bf16)
        xpart = sb("xpart", [P, 2, PARTS, BLK, COLS], fp32)
        zu = sb("zu", [P, BODY, COLS, 2], fp32)
        zpart = sb("zpart", [P, 2, BLK, PARTS, COLS], fp32)
        hist = sb("hist", [P, BODY, PARTS, COLS], fp32)
        ybuf = sb("ybuf", [P, 2, BLK, COLS], fp32)
        aux_s = sb("aux_s", [P, AUX_COLS], fp32)

        set_bank = [pb(f"set_bank{j}") for j in chunks]
        aux = [aux_s if j == 1 else pb(f"aux_bank{j}") for j in chunks]
        in_bank = pb("in_bank")

        loaded_w = {m: [sem(f"loaded_w{m}{j}") for j in chunks] for m in "zh"}
        loaded_c = sem("loaded_c")
        loaded_x = [sem(f"loaded_x{i}") for i in range(2)]
        stored_y = [sem(f"stored_y{i}") for i in range(2)]
        zeroed = sem("zeroed")
        ident_ready = sem("ident_ready")
        w_rests = sem("w_rests")
        w_part01 = sem("w_part01")
        w_part2 = {m: sem(f"w{m}_part2") for m in "zh"}
        leak_link = sem("leak_link")
        aux_clear = sem("aux_clear")
        x_rest = sem("x_rest")
        x_split = sem("x_split")
        in_mm = sem("in_mm")
        in_full = sem("in_full")
        in_rest = sem("in_rest")
        in_split = sem("in_split")
        z_copied = sem("z_copied")
        leaked = sem("leaked")
        summed_y = sem("summed_y")
        gate_mm = [sem(f"gate_mm{j}") for j in chunks]
        pre_sum = [sem(f"pre_sum{j}") for j in chunks]
        gated = [sem(f"gated{j}") for j in chunks]
        mixed = [sem(f"mixed{j}") for j in chunks]
        h_full = [sem(f"h_full{j}") for j in chunks]
        h0_rest = sem("h0_rest")
        h_rest = [sem(f"h_rest{j}") for j in chunks]
        h_split = [sem(f"h_split{j}") for j in chunks]

        block = ctx.enter_context(nc.Block())

        def upper(ap):
            return ap.bitcast(bf16)[..., 1::2]

        def part_sets(j):
            return set_bank[j][:, 0:PARTS * B].rearrange("p (a c) -> p a c", a=PARTS)

        def gate_pairs(j):
            return aux[j][:, GATE_AT:GATE_AT + 2 * B]

        def arg_pairs(j):
            return aux[j][:, ARG_AT:ARG_AT + 2 * B]

        def w_block(m, w, j, k):
            return w_part[m][:, w, j, k * P:(k + 1) * P]

        def x_steps(at):
            return bass.ds(at * COLS, BLK * COLS)

        def input_product(s):
            m = (s + CH) % BLK
            return m // CH, m % CH, 1 if s + CH < BLK else 2

        def has_block(last, parity, ahead):
            return not last or parity + ahead < 2

        def bodies(engine_type, eng, emit):
            with nc.Fori(0, BODIES - 1, engines=(engine_type,), hint_back_edge=True) as n:
                emit(eng.snap(n * BODY), eng.snap(n * 16), False)
            emit((BODIES - 1) * BODY, (BODIES - 1) * 16, True)

        @block.sync
        def _(sp):
            def load_x(t, parity):
                sp.dma_start(xpart[:, parity, 0], x[:, x_steps(t)].rearrange("p (t c) -> p t c", c=COLS))\
                    .then_inc(loaded_x[parity], 16)

            sp.dma_start(w_whole["z"][:, 0], wz[:, 0:CH * P]).then_inc(loaded_w["z"][0], 16)
            load_x(0, 0)
            for m, w, first in (("z", wz, 1), ("h", wh, 0)):
                for j in range(first, CH):
                    sp.dma_start(w_whole[m][:, j], w[:, j * CH * P:(j + 1) * CH * P]).then_inc(loaded_w[m][j], 16)
            load_x(BLK, 1)

            def emit(t, dmas, last):
                for parity in range(2):
                    t_blk = t + parity * BLK
                    if has_block(last, parity, 2):
                        sp.wait_ge(in_mm, t_blk + BLK)
                        sp.wait_ge(z_copied, t_blk + BLK)
                        load_x(t_blk + 2 * BLK, parity)
                    sp.wait_ge(summed_y, t_blk + 2 * BLK)
                    sp.dma_start(y[:, x_steps(t_blk)].rearrange("p (t c) -> p t c", c=COLS), ybuf[:, parity])\
                        .then_inc(stored_y[parity], 16)

            bodies(mybir.EngineType.SP, sp, emit)
            for parity in range(2):
                sp.wait_ge(stored_y[parity], 16 * (1 + BODIES))

        @block.gpsimd
        def _(pool):
            pool.memset(ident[:], 0.0).then_inc(zeroed, 1)
            pool.memset(leak[:], 0.0).then_inc(leak_link, 1)
            for parity in range(2):
                pool.memset(ybuf[:, parity, 0], 0.0).then_inc(stored_y[parity], 16)
            pool.memset(ybuf[:, 0, 1], 0.0).then_inc(summed_y, BLK)
            pool.wait_ge(zeroed, 1)
            pool.affine_select(out=ident[:], in_=ident[:], compare_op=ALU.not_equal, fill=1.0, base=0,
                               pattern=[[-1, P]], channel_multiplier=1).then_inc(ident_ready, 1)

            pool.wait_ge(loaded_c, 48)
            pool.wait_ge(leak_link, 1)
            for j in chunks:
                pool.tensor_scalar(leak[:, cols(j)], leak[:, cols(j)], alpha_s[:, j:j + 1], None, ALU.add)\
                    .then_inc(leak_link, 1)
            pool.wait_ge(leak_link, 1 + CH)
            pool.tensor_scalar(leak[:], leak[:], -1.0, 1.0, ALU.mult, ALU.add).then_inc(leak_link, 1)
            pool.tensor_tensor(hist[:, BODY - 1, 1, :], hist[:, BODY - 1, 0, :], upper(hist[:, BODY - 1, 0, :]),
                               ALU.subtract).then_inc(h0_rest, 1)
            pool.wait_ge(h0_rest, 1)
            for j in chunks:
                rest = hist[:, BODY - 1, 1, cols(j)]
                pool.tensor_tensor(hist[:, BODY - 1, 2, cols(j)], rest, upper(rest), ALU.subtract)\
                    .then_inc(h_split[j], 1)
            pool.wait_ge(leak_link, 2 + CH)
            pool.tensor_tensor(zu[:, 0, :, 1], hist[:, BODY - 1, 0, :], leak[:], ALU.mult).then_inc(leaked, 1)
            for j in chunks:
                pool.wait_ge(w_rests, CH + j + 1)
                pool.tensor_tensor(w_part["h"][:, 2, j], w_rest["h"][:, j], upper(w_rest["h"][:, j]), ALU.subtract)\
                    .then_inc(w_part2["h"], 1)

            def split_input(parity, j, a):
                before = zpart[:, parity, :, a - 1, cols(j)]
                pool.tensor_tensor(zpart[:, parity, :, a, cols(j)], before, upper(before), ALU.subtract)\
                    .then_inc(in_rest if a == 1 else in_split, 4)

            def add_y(parity, q):
                at = parity * BLK + q * PIECE
                pool.tensor_tensor(ybuf[:, parity, q * PIECE:(q + 1) * PIECE, :],
                                   zu[:, at:at + PIECE, :, 0], hist[:, at:at + PIECE, 0, :],
                                   ALU.add).then_inc(summed_y, 4)

            def emit(t, dmas, last):
                for s_body in range(BODY):
                    parity, s = divmod(s_body, BLK)
                    now = t + s_body
                    q, r = divmod(s, PIECE)
                    if last and s_body == BODY - 1:
                        for j in chunks:
                            pool.wait_ge(h_full[j], now + 1)
                    elif r != 2:
                        pool.wait_ge(leaked, now + 2)
                    if r == 0 and has_block(last, parity, 1):
                        pool.wait_ge(in_full, now + BLK + 4)
                        split_input(1 - parity, q, 1)
                    if r == 1 and has_block(last, parity, 1):
                        pool.wait_ge(in_rest, now + BLK + 3)
                        split_input(1 - parity, q, 2)
                    if r == PIECE - 1:
                        if q == 0:
                            pool.wait_ge(stored_y[parity], dmas + 16)
                        add_y(parity, q)

            bodies(mybir.EngineType.Pool, pool, emit)

        @block.tensor
        def _(pe):
            def multiply_input(bank, parity, j, k):
                for w in range(PARTS):
                    for a in range(PARTS):
                        mm = pe.matmul(bank[:, 0:BLK * B], w_block("z", w, j, k),
                                       upper(xpart[:, parity, a, :, cols(k)]),
                                       start=(k == w == a == 0), stop=(k == CH - 1 and w == a == PARTS - 1))
                mm.then_inc(in_mm, 1)

            def open_step(slot):
                parity, s = divmod(slot, BLK)
                for j in chunks:
                    pe.matmul(part_sets(j), ident[:], upper(zpart[:, parity, s, :, cols(j)]),
                              start=True, stop=False, skip_group_check=True)

            pe.wait_ge(ident_ready, 1)
            for _ in range(WARM_UP):
                pe.matmul(in_bank[:, 0:P], ident[:], ident[:], start=True, stop=True)
            for n in range(CH + 1):
                parity, j = divmod(n, CH)
                if parity == 0:
                    pe.wait_ge(w_part01, j + 1)
                    pe.wait_ge(w_part2["z"], j + 1)
                if j == 0:
                    pe.wait_ge(x_split, BLK * (parity + 1))
                for k in chunks:
                    multiply_input(in_bank if parity else set_bank[j], parity, j, k)
            pe.wait_ge(in_split, BLK)
            open_step(0)
            pe.wait_ge(w_part01, 2 * CH)
            pe.wait_ge(w_part2["h"], CH)

            def emit(t, dmas, last):
                for s_body in range(BODY):
                    parity, s = divmod(s_body, BLK)
                    before = (s_body - 1) % BODY
                    now = t + s_body
                    arrived = 0
                    for i, (j, k, w) in enumerate(PASSES):
                        if k == arrived:
                            arrived += 1
                            pe.wait_ge(h_split[k], now + 1)
                        mm = pe.matmul(part_sets(j), w_block("h", w, j, k), upper(hist[:, before, :, cols(k)]),
                                       start=False, stop=(i == FINAL[j]), skip_group_check=True)
                        if i == FINAL[j]:
                            mm.then_inc(gate_mm[j], 1)
                    j, k, ahead = input_product(s)
                    if has_block(last, parity, ahead):
                        if k == 0:
                            pe.wait_ge(in_full, now + BLK + 4)
                            if j == 0:
                                pe.wait_ge(x_split, now + CH + 2 * BLK)
                        multiply_input(in_bank, (parity + ahead) % 2, j, k)
                    if not (last and s_body == BODY - 1):
                        if s == BLK - 1:
                            pe.wait_ge(in_split, now + 1 + BLK)
                        for j in chunks:
                            pe.wait_ge(pre_sum[j], now + 1)
                        open_step((s_body + 1) % BODY)

            bodies(mybir.EngineType.PE, pe, emit)

        @block.scalar
        def _(act):
            act.preload_act_table(ACT.Sigmoid)
            act.dma_start(alpha_s[:], alpha).then_inc(loaded_c, 16)
            act.dma_start(hist[:, BODY - 1, 0], h0).then_inc(loaded_c, 16)
            act.dma_start(bias_s[:], bias).then_inc(loaded_c, 16)

            def evacuate(bank, parity, j):
                nc.scalar.activation(zpart[:, parity, :, 0, cols(j)],
                                     bank[:, 0:BLK * B].rearrange("p (t b) -> p t b", b=B),
                                     ACT.Identity, bias=bias_s[:, j:j + 1]).then_inc(in_full, 4)

            def copy_z(parity, q):
                at = parity * BLK + q * PIECE
                nc.scalar.copy(zu[:, at:at + PIECE, :, 0],
                               xpart[:, parity, 0, q * PIECE:(q + 1) * PIECE, :]).then_inc(z_copied, 4)

            def copy_w(m, j):
                n = j + CH * "zh".index(m)
                act.wait_ge(loaded_w[m][j], 16)
                nc.scalar.copy(w_part[m][:, 0, j], upper(w_whole[m][:, j]))
                act.wait_ge(w_rests, n + 1)
                nc.scalar.copy(w_part[m][:, 1, j], upper(w_rest[m][:, j])).then_inc(w_part01, 1)

            for j in chunks:
                copy_w("z", j)
            act.wait_ge(loaded_c, 48)
            for n in range(CH + 1):
                act.wait_ge(in_mm, (n + 1) * CH)
                evacuate(set_bank[n] if n < CH else in_bank, n // CH, n % CH)
                if n < CH:
                    copy_w("h", n)
                    copy_z(0, n)

            def sigmoid(j, now):
                act.wait_ge(pre_sum[j], now + 1)
                nc.scalar.activation(gate_pairs(j)[:, 1::2], aux[j][:, SUM_AT:SUM_AT + B], ACT.Sigmoid)\
                    .then_inc(gated[j], 1)

            def tanh(j, slot, now):
                act.wait_ge(mixed[j], now + 1)
                nc.scalar.activation(hist[:, slot, 0, cols(j)], arg_pairs(j)[:, 1::2], ACT.Tanh)\
                    .then_inc(h_full[j], 1)

            def emit(t, dmas, last):
                for s_body in range(BODY):
                    parity, s = divmod(s_body, BLK)
                    now = t + s_body
                    sigmoid(0, now)
                    sigmoid(1, now)
                    sigmoid(2, now)
                    tanh(0, s_body, now)
                    sigmoid(3, now)
                    tanh(1, s_body, now)
                    tanh(2, s_body, now)
                    tanh(3, s_body, now)
                    j, k, ahead = input_product(s)
                    if k == CH - 1 and has_block(last, parity, ahead):
                        act.wait_ge(in_mm, now + 1 + BLK + CH)
                        evacuate(in_bank, (parity + ahead) % 2, j)
                    q, r = divmod(s, PIECE)
                    if r == 1 and has_block(last, parity, 1):
                        if q == 0:
                            act.wait_ge(loaded_x[1 - parity], dmas + parity * 16 + 16)
                        act.wait_ge(summed_y, now - 1 + PIECE)
                        copy_z(1 - parity, q)

            bodies(mybir.EngineType.Activation, act, emit)

        @block.vector
        def _(dve):
            def split_w(m, j):
                n = j + CH * "zh".index(m)
                dve.wait_ge(loaded_w[m][j], 16)
                dve.tensor_tensor(w_rest[m][:, j], w_whole[m][:, j], upper(w_whole[m][:, j]), ALU.subtract)\
                    .then_inc(w_rests, 1)
                if m == "z":
                    dve.wait_ge(w_rests, n + 1)
                    dve.tensor_tensor(w_part[m][:, 2, j], w_rest[m][:, j], upper(w_rest[m][:, j]), ALU.subtract)\
                        .then_inc(w_part2[m], 1)

            def split_x(parity, pieces, a):
                steps = slice(pieces[0] * PIECE, (pieces[-1] + 1) * PIECE)
                before = xpart[:, parity, a - 1, steps, :]
                dve.tensor_tensor(xpart[:, parity, a, steps, :], before, upper(before), ALU.subtract)\
                    .then_inc(x_rest if a == 1 else x_split, 4 * len(pieces))

            def second_part(j, slot):
                whole = hist[:, slot, 0, cols(j)]
                dve.tensor_tensor(hist[:, slot, 1, cols(j)], whole, upper(whole), ALU.subtract).then_inc(h_rest[j], 1)

            def third_part(j, slot, count):
                dve.wait_ge(h_rest[j], count)
                rest = hist[:, slot, 1, cols(j)]
                dve.tensor_tensor(hist[:, slot, 2, cols(j)], rest, upper(rest), ALU.subtract).then_inc(h_split[j], 1)

            def leak_times_h(slot_in, slot_out):
                dve.tensor_tensor(zu[:, slot_out, :, 1], hist[:, slot_in, 0, :], leak[:], ALU.mult).then_inc(leaked, 1)

            for j in chunks:
                dve.memset(gate_pairs(j), 0.0).then_inc(aux_clear, 1)

            def split_block_x(parity):
                dve.wait_ge(loaded_x[parity], 16)
                split_x(parity, chunks, 1)
                dve.wait_ge(x_rest, BLK * (parity + 1))
                split_x(parity, chunks, 2)

            def split_input(j):
                for a in (1, 2):
                    dve.wait_ge(in_full if a == 1 else in_rest, 4 * (j + 1))
                    before = zpart[:, 0, :, a - 1, cols(j)]
                    dve.tensor_tensor(zpart[:, 0, :, a, cols(j)], before, upper(before), ALU.subtract)\
                        .then_inc(in_rest if a == 1 else in_split, 4)

            split_w("z", 0)
            split_block_x(0)
            for j in range(1, CH):
                split_w("z", j)
            split_w("h", 0)
            split_w("h", 1)
            split_input(0)
            split_w("h", 2)
            split_block_x(1)
            split_input(1)
            split_w("h", 3)
            split_input(2)
            split_input(3)
            dve.wait_ge(aux_clear, CH)
            dve.wait_ge(z_copied, BLK)

            def sum_sets(j, now):
                dve.wait_ge(gate_mm[j], now + 1)
                dve.tensor_reduce(aux[j][:, SUM_AT:SUM_AT + B], part_sets(j).rearrange("p a c -> p c a"),
                                  AX.X, ALU.add).then_inc(pre_sum[j], 1)

            def mix(j, slot, now):
                dve.wait_ge(gated[j], now + 1)
                if j == 0:
                    dve.wait_ge(leaked, now + 1)
                dve.tensor_tensor_scan(arg_pairs(j), gate_pairs(j),
                                       zu[:, slot, cols(j), :].rearrange("p c two -> p (c two)"),
                                       0.0, ALU.mult, ALU.add).then_inc(mixed[j], 1)

            def emit(t, dmas, last):
                for slot in range(BODY):
                    parity, s = divmod(slot, BLK)
                    now = t + slot
                    end = last and slot == BODY - 1

                    def rest(j):
                        if not end:
                            dve.wait_ge(h_full[j], now + 1)
                            second_part(j, slot)

                    def third(j):
                        if not end:
                            third_part(j, slot, now + 1)

                    sum_sets(0, now)
                    sum_sets(1, now)
                    sum_sets(2, now)
                    mix(0, slot, now)
                    sum_sets(3, now)
                    mix(1, slot, now)
                    mix(2, slot, now)
                    rest(0)
                    mix(3, slot, now)
                    third(0)
                    rest(1)
                    rest(2)
                    third(1)
                    rest(3)
                    third(2)
                    third(3)
                    if s == BLK - 1 and not end:
                        dve.wait_ge(z_copied, now + 1 + BLK)
                    if not end:
                        leak_times_h(slot, (slot + 1) % BODY)
                    q, r = divmod(s, PIECE)
                    if has_block(last, parity, 2) and q in (1, 2):
                        if q == 1 and r == 0:
                            dve.wait_ge(loaded_x[parity], dmas + 32)
                        if q == 2:
                            dve.wait_ge(x_rest, now - s + 2 * BLK + 4 * (r + 1))
                        split_x(parity, [r], q)

            bodies(mybir.EngineType.DVE, dve, emit)


def kernel(x, cond_1024, L0_cond_W, L0_cond_b, L0_cond_alpha):
    import numpy as np
    import concourse.bacc as bacc
    from concourse.bass_utils import run_bass_kernel_spmd

    P = 128
    x, h0, W = (np.asarray(a) for a in (x, cond_1024, L0_cond_W))
    bias, alpha = np.asarray(L0_cond_b), np.asarray(L0_cond_alpha)
    B, T, D = x.shape
    CH = D // P

    def blocks(w):
        return np.ascontiguousarray(w.reshape(CH, P, CH, P).transpose(3, 0, 2, 1).reshape(P, CH * CH * P))

    arrays = {
        "x_dram": np.ascontiguousarray(x.reshape(B, T, CH, P).transpose(3, 1, 2, 0).reshape(P, T * CH * B)),
        "h0_dram": np.ascontiguousarray(h0.reshape(B, CH, P).transpose(2, 1, 0).reshape(P, CH * B)),
        "wh_dram": blocks(W[:, :D]),
        "wz_dram": blocks(W[:, D:]),
        "bias_dram": np.ascontiguousarray(bias.reshape(CH, P).T),
        "alpha_dram": np.ascontiguousarray(alpha.reshape(CH, P).T),
    }
    nc = bacc.Bacc("TRN2", target_bir_lowering=False, num_devices=1)
    args = [nc.dram_tensor(name, a.shape, mybir.dt.from_np(a.dtype), kind="ExternalInput").ap()
            for name, a in arrays.items()]
    y = nc.dram_tensor("y_dram", [P, T * CH * B], mybir.dt.float32, kind="ExternalOutput").ap()
    cond_resid_kernel(nc, *args, y)
    out = run_bass_kernel_spmd(nc, [arrays], core_ids=[0]).results[0]["y_dram"]
    return np.ascontiguousarray(np.asarray(out).reshape(P, T, CH, B).transpose(3, 1, 2, 0).reshape(B, T, D))
```
